# Optimizing a Trainium2 kernel written in Bass

```python
import numpy as np
import jax
import jax.numpy as jnp

def _softmax(x, axis=-1):
    return jax.nn.softmax(x, axis=axis)

def _gelu(x):
    return jax.nn.gelu(x, approximate=True)

def _silu(x):
    return jax.nn.silu(x)

def _sigmoid(x):
    return jax.nn.sigmoid(x)

def _layernorm(x, axis=-1, eps=1e-05):
    m = jnp.mean(x, axis=axis, keepdims=True)
    v = jnp.var(x, axis=axis, keepdims=True)
    return (x - m) / jnp.sqrt(v + eps)

def _scatter_add(tgt, idx, src, axis=0):
    return tgt.at[idx].add(src)

def _segment_sum(src, seg, n):
    return jax.ops.segment_sum(src, seg, n)
kernel_name = 'mk_xattn_seq_d2_seqx_r4_306c3e'

def setup_inputs(seed: int=0):
    np.random.seed(seed)
    _w = jnp.asarray

    def _rec_inputs():
        import jax
        import jax.numpy as jnp
        _rk = jax.random.key(seed)
        x = -0.0002928 + 1 * jax.random.normal(jax.random.fold_in(_rk, 1), (128, 128, 256), jnp.float32)
        _lenS = 128 - jax.random.randint(jax.random.fold_in(_rk, 7), (128,), 0, max(1, 128 // 4) + 1, jnp.int32)
        _lenS2 = 128 - jax.random.randint(jax.random.fold_in(_rk, 8), (128,), 0, max(1, 128 // 4) + 1, jnp.int32)
        _ctx_1024P = jax.random.normal(jax.random.fold_in(_rk, 11), (128, 16, 256), jnp.float32)
        _ctx_1024c = jax.random.dirichlet(jax.random.fold_in(_rk, 511), 0.3 * jnp.ones((16,), jnp.float32), (128, 128))
        _ctx_1024t = jnp.einsum('bsk,bkd->bsd', _ctx_1024c, _ctx_1024P)
        _ctx_1024t = _ctx_1024t * jax.lax.rsqrt(jnp.mean(jnp.square(_ctx_1024t)) + 1e-12) * 0.953939
        ctx_1024 = -1.39393e-06 + 0.999914 * (_ctx_1024t + 0.3 * jax.random.normal(jax.random.fold_in(_rk, 611), (128, 128, 256), jnp.float32))
        return (x, ctx_1024)
    x, ctx_1024 = _rec_inputs()

    def _L0_xattn_setup():
        import jax, jax.numpy as jnp
        import numpy as np
        B, LX, LY = (2, 512, 512)
        E, H = (256, 16)
        HD = E // H
        FF = 1024
        EPS = 1e-05

        def _rope_tables(L, d):
            inv = 1.0 / 10000.0 ** (jnp.arange(0, d, 2, dtype=jnp.float32) / d)
            t = jnp.arange(L, dtype=jnp.float32)
            f = jnp.outer(t, inv)
            return (jnp.cos(f), jnp.sin(f))

        def _apply_rope(x, cos, sin):
            d2 = x.shape[-1] // 2
            x1, x2 = (x[..., :d2], x[..., d2:])
            c = cos[None, :, None, :]
            s = sin[None, :, None, :]
            return jnp.concatenate([x1 * c - x2 * s, x2 * c + x1 * s], axis=-1)

        def _ln(x, g, b):
            m = jnp.mean(x, axis=-1, keepdims=True)
            v = jnp.var(x, axis=-1, keepdims=True)
            return (x - m) / jnp.sqrt(v + EPS) * g + b

        def _attn(q, k, v, causal):
            s = jnp.einsum('blhd,bmhd->bhlm', q, k)
            if causal:
                Lq, Lk = (s.shape[2], s.shape[3])
                mask = jnp.tril(jnp.ones((Lq, Lk), dtype=bool))
                s = jnp.where(mask, s, -jnp.inf)
            p = jax.nn.softmax(s, axis=-1)
            return jnp.einsum('bhlm,bmhd->blhd', p, v)

        def _forward(x, y, ln1_g, ln1_b, sa_wq, sa_bq, sa_wk, sa_bk, sa_wv, sa_bv, sa_wo, sa_bo, ln2_g, ln2_b, ca_wq, ca_bq, ca_wk, ca_bk, ca_wv, ca_bv, ca_wo, ca_bo, ln3_g, ln3_b, fc1_w, fc1_b, fc2_w, fc2_b):
            Bx, Lx, _ = x.shape
            Ly = y.shape[1]
            cos, sin = _rope_tables(max(Lx, Ly), HD)
            scale = HD ** (-0.5)
            h = _ln(x, ln1_g, ln1_b)
            q = (h @ sa_wq + sa_bq).reshape(Bx, Lx, H, HD) * scale
            k = (h @ sa_wk + sa_bk).reshape(Bx, Lx, H, HD)
            v = (h @ sa_wv + sa_bv).reshape(Bx, Lx, H, HD)
            q = _apply_rope(q, cos[:Lx], sin[:Lx])
            k = _apply_rope(k, cos[:Lx], sin[:Lx])
            a = _attn(q, k, v, causal=True).reshape(Bx, Lx, E)
            x = x + (a @ sa_wo + sa_bo)
            h = _ln(x, ln2_g, ln2_b)
            q = (h @ ca_wq + ca_bq).reshape(Bx, Lx, H, HD) * scale
            k = (y @ ca_wk + ca_bk).reshape(Bx, Ly, H, HD)
            v = (y @ ca_wv + ca_bv).reshape(Bx, Ly, H, HD)
            q = _apply_rope(q, cos[:Lx], sin[:Lx])
            k = _apply_rope(k, cos[:Ly], sin[:Ly])
            a = _attn(q, k, v, causal=False).reshape(Bx, Lx, E)
            x = x + (a @ ca_wo + ca_bo)
            h = _ln(x, ln3_g, ln3_b)
            return x + (jax.nn.gelu(h @ fc1_w + fc1_b) @ fc2_w + fc2_b)
        key = jax.random.key(seed)
        ks = jax.random.split(key, 16)

        def w(k, *s):
            return jax.random.normal(k, s, jnp.float32) * 0.02
        z = lambda *s: jnp.zeros(s, jnp.float32)
        o = lambda *s: jnp.ones(s, jnp.float32)
        return {'x': jax.random.normal(ks[0], (B, LX, E), jnp.float32), 'y': jax.random.normal(ks[1], (B, LY, E), jnp.float32), 'ln1_g': o(E), 'ln1_b': z(E), 'sa_wq': w(ks[2], E, E), 'sa_bq': z(E), 'sa_wk': w(ks[3], E, E), 'sa_bk': z(E), 'sa_wv': w(ks[4], E, E), 'sa_bv': z(E), 'sa_wo': w(ks[5], E, E), 'sa_bo': z(E), 'ln2_g': o(E), 'ln2_b': z(E), 'ca_wq': w(ks[6], E, E), 'ca_bq': z(E), 'ca_wk': w(ks[7], E, E), 'ca_bk': z(E), 'ca_wv': w(ks[8], E, E), 'ca_bv': z(E), 'ca_wo': w(ks[9], E, E), 'ca_bo': z(E), 'ln3_g': o(E), 'ln3_b': z(E), 'fc1_w': w(ks[10], E, FF), 'fc1_b': z(FF), 'fc2_w': w(ks[11], FF, E), 'fc2_b': z(E)}
    _L0_xattn_all = _L0_xattn_setup()
    _L0_xattn_in = {k: v for k, v in _L0_xattn_all.items() if k in ('ln1_g', 'ln1_b', 'sa_wq', 'sa_bq', 'sa_wk', 'sa_bk', 'sa_wv', 'sa_bv', 'sa_wo', 'sa_bo', 'ln2_g', 'ln2_b', 'ca_wq', 'ca_bq', 'ca_wk', 'ca_bk', 'ca_wv', 'ca_bv', 'ca_wo', 'ca_bo', 'ln3_g', 'ln3_b', 'fc1_w', 'fc1_b', 'fc2_w', 'fc2_b')}
    del _L0_xattn_all

    def _L1_xattn_setup():
        import jax, jax.numpy as jnp
        import numpy as np
        HIDDEN_NUMS = 128
        key = jax.random.key(seed)
        k1, k2, k3 = jax.random.split(key, 3)
        B, S, T, H2 = (32, 256, 64, 2 * HIDDEN_NUMS)
        target_hidden_states = jax.random.normal(k1, (B, T, H2), dtype=jnp.float32)
        hidden_states = jax.random.normal(k2, (B, S, H2), dtype=jnp.float32)
        trans_W = jax.random.uniform(k3, (4 * HIDDEN_NUMS, H2), dtype=jnp.float32, minval=-0.01, maxval=0.01)
        trans_b = jnp.zeros((H2,), dtype=jnp.float32)
        return {'target_hidden_states': target_hidden_states, 'hidden_states': hidden_states, 'trans_W': trans_W, 'trans_b': trans_b}
    _L1_xattn_all = _L1_xattn_setup()
    _L1_xattn_in = {k: v for k, v in _L1_xattn_all.items() if k in ('trans_W', 'trans_b')}
    del _L1_xattn_all
    return {'x': x, 'ctx_1024': ctx_1024, 'L0_xattn_ln1_g': _L0_xattn_in['ln1_g'], 'L0_xattn_ln1_b': _L0_xattn_in['ln1_b'], 'L0_xattn_sa_wq': _L0_xattn_in['sa_wq'], 'L0_xattn_sa_bq': _L0_xattn_in['sa_bq'], 'L0_xattn_sa_wk': _L0_xattn_in['sa_wk'], 'L0_xattn_sa_bk': _L0_xattn_in['sa_bk'], 'L0_xattn_sa_wv': _L0_xattn_in['sa_wv'], 'L0_xattn_sa_bv': _L0_xattn_in['sa_bv'], 'L0_xattn_sa_wo': _L0_xattn_in['sa_wo'], 'L0_xattn_sa_bo': _L0_xattn_in['sa_bo'], 'L0_xattn_ln2_g': _L0_xattn_in['ln2_g'], 'L0_xattn_ln2_b': _L0_xattn_in['ln2_b'], 'L0_xattn_ca_wq': _L0_xattn_in['ca_wq'], 'L0_xattn_ca_bq': _L0_xattn_in['ca_bq'], 'L0_xattn_ca_wk': _L0_xattn_in['ca_wk'], 'L0_xattn_ca_bk': _L0_xattn_in['ca_bk'], 'L0_xattn_ca_wv': _L0_xattn_in['ca_wv'], 'L0_xattn_ca_bv': _L0_xattn_in['ca_bv'], 'L0_xattn_ca_wo': _L0_xattn_in['ca_wo'], 'L0_xattn_ca_bo': _L0_xattn_in['ca_bo'], 'L0_xattn_ln3_g': _L0_xattn_in['ln3_g'], 'L0_xattn_ln3_b': _L0_xattn_in['ln3_b'], 'L0_xattn_fc1_w': _L0_xattn_in['fc1_w'], 'L0_xattn_fc1_b': _L0_xattn_in['fc1_b'], 'L0_xattn_fc2_w': _L0_xattn_in['fc2_w'], 'L0_xattn_fc2_b': _L0_xattn_in['fc2_b'], 'L1_xattn_trans_W': _L1_xattn_in['trans_W'], 'L1_xattn_trans_b': _L1_xattn_in['trans_b']}

def reference(x, ctx_1024, L0_xattn_ln1_g, L0_xattn_ln1_b, L0_xattn_sa_wq, L0_xattn_sa_bq, L0_xattn_sa_wk, L0_xattn_sa_bk, L0_xattn_sa_wv, L0_xattn_sa_bv, L0_xattn_sa_wo, L0_xattn_sa_bo, L0_xattn_ln2_g, L0_xattn_ln2_b, L0_xattn_ca_wq, L0_xattn_ca_bq, L0_xattn_ca_wk, L0_xattn_ca_bk, L0_xattn_ca_wv, L0_xattn_ca_bv, L0_xattn_ca_wo, L0_xattn_ca_bo, L0_xattn_ln3_g, L0_xattn_ln3_b, L0_xattn_fc1_w, L0_xattn_fc1_b, L0_xattn_fc2_w, L0_xattn_fc2_b, L1_xattn_trans_W, L1_xattn_trans_b):
    import jax
    import jax.numpy as jnp

    def _L0_xattn_ref(x, y, ln1_g, ln1_b, sa_wq, sa_bq, sa_wk, sa_bk, sa_wv, sa_bv, sa_wo, sa_bo, ln2_g, ln2_b, ca_wq, ca_bq, ca_wk, ca_bk, ca_wv, ca_bv, ca_wo, ca_bo, ln3_g, ln3_b, fc1_w, fc1_b, fc2_w, fc2_b):
        import jax, jax.numpy as jnp
        import numpy as np
        B, LX, LY = (2, 512, 512)
        E, H = (256, 16)
        HD = E // H
        FF = 1024
        EPS = 1e-05

        def _rope_tables(L, d):
            inv = 1.0 / 10000.0 ** (jnp.arange(0, d, 2, dtype=jnp.float32) / d)
            t = jnp.arange(L, dtype=jnp.float32)
            f = jnp.outer(t, inv)
            return (jnp.cos(f), jnp.sin(f))

        def _apply_rope(x, cos, sin):
            d2 = x.shape[-1] // 2
            x1, x2 = (x[..., :d2], x[..., d2:])
            c = cos[None, :, None, :]
            s = sin[None, :, None, :]
            return jnp.concatenate([x1 * c - x2 * s, x2 * c + x1 * s], axis=-1)

        def _ln(x, g, b):
            m = jnp.mean(x, axis=-1, keepdims=True)
            v = jnp.var(x, axis=-1, keepdims=True)
            return (x - m) / jnp.sqrt(v + EPS) * g + b

        def _attn(q, k, v, causal):
            s = jnp.einsum('blhd,bmhd->bhlm', q, k)
            if causal:
                Lq, Lk = (s.shape[2], s.shape[3])
                mask = jnp.tril(jnp.ones((Lq, Lk), dtype=bool))
                s = jnp.where(mask, s, -jnp.inf)
            p = jax.nn.softmax(s, axis=-1)
            return jnp.einsum('bhlm,bmhd->blhd', p, v)

        def _forward(x, y, ln1_g, ln1_b, sa_wq, sa_bq, sa_wk, sa_bk, sa_wv, sa_bv, sa_wo, sa_bo, ln2_g, ln2_b, ca_wq, ca_bq, ca_wk, ca_bk, ca_wv, ca_bv, ca_wo, ca_bo, ln3_g, ln3_b, fc1_w, fc1_b, fc2_w, fc2_b):
            Bx, Lx, _ = x.shape
            Ly = y.shape[1]
            cos, sin = _rope_tables(max(Lx, Ly), HD)
            scale = HD ** (-0.5)
            h = _ln(x, ln1_g, ln1_b)
            q = (h @ sa_wq + sa_bq).reshape(Bx, Lx, H, HD) * scale
            k = (h @ sa_wk + sa_bk).reshape(Bx, Lx, H, HD)
            v = (h @ sa_wv + sa_bv).reshape(Bx, Lx, H, HD)
            q = _apply_rope(q, cos[:Lx], sin[:Lx])
            k = _apply_rope(k, cos[:Lx], sin[:Lx])
            a = _attn(q, k, v, causal=True).reshape(Bx, Lx, E)
            x = x + (a @ sa_wo + sa_bo)
            h = _ln(x, ln2_g, ln2_b)
            q = (h @ ca_wq + ca_bq).reshape(Bx, Lx, H, HD) * scale
            k = (y @ ca_wk + ca_bk).reshape(Bx, Ly, H, HD)
            v = (y @ ca_wv + ca_bv).reshape(Bx, Ly, H, HD)
            q = _apply_rope(q, cos[:Lx], sin[:Lx])
            k = _apply_rope(k, cos[:Ly], sin[:Ly])
            a = _attn(q, k, v, causal=False).reshape(Bx, Lx, E)
            x = x + (a @ ca_wo + ca_bo)
            h = _ln(x, ln3_g, ln3_b)
            return x + (jax.nn.gelu(h @ fc1_w + fc1_b) @ fc2_w + fc2_b)
        return _forward(x, y, ln1_g, ln1_b, sa_wq, sa_bq, sa_wk, sa_bk, sa_wv, sa_bv, sa_wo, sa_bo, ln2_g, ln2_b, ca_wq, ca_bq, ca_wk, ca_bk, ca_wv, ca_bv, ca_wo, ca_bo, ln3_g, ln3_b, fc1_w, fc1_b, fc2_w, fc2_b)

    def _L1_xattn_ref(target_hidden_states, hidden_states, trans_W, trans_b):
        import jax, jax.numpy as jnp
        import numpy as np
        HIDDEN_NUMS = 128
        scores = jnp.einsum('bsd,btd->bst', hidden_states, target_hidden_states)
        attn = jax.nn.softmax(scores, axis=-1)
        ti = jnp.einsum('bst,btd->bsd', attn, target_hidden_states)
        cat = jnp.concatenate([hidden_states, ti], axis=-1)
        hi_new = jnp.tanh(jnp.einsum('bsf,fd->bsd', cat, trans_W) + trans_b)
        return hi_new + hidden_states
    x = _L0_xattn_ref(x, ctx_1024, L0_xattn_ln1_g, L0_xattn_ln1_b, L0_xattn_sa_wq, L0_xattn_sa_bq, L0_xattn_sa_wk, L0_xattn_sa_bk, L0_xattn_sa_wv, L0_xattn_sa_bv, L0_xattn_sa_wo, L0_xattn_sa_bo, L0_xattn_ln2_g, L0_xattn_ln2_b, L0_xattn_ca_wq, L0_xattn_ca_bq, L0_xattn_ca_wk, L0_xattn_ca_bk, L0_xattn_ca_wv, L0_xattn_ca_bv, L0_xattn_ca_wo, L0_xattn_ca_bo, L0_xattn_ln3_g, L0_xattn_ln3_b, L0_xattn_fc1_w, L0_xattn_fc1_b, L0_xattn_fc2_w, L0_xattn_fc2_b)
    x = _L1_xattn_ref(ctx_1024, x, L1_xattn_trans_W, L1_xattn_trans_b)
    return x

_drawn_inputs = setup_inputs


def setup_inputs(seed=0):
    import zlib

    import numpy as np

    out = dict(_drawn_inputs(seed))
    spreads = {'L0_xattn_ln1_g': (1.0, 0.6),
     'L0_xattn_ln1_b': (0.0, 0.789),
     'L0_xattn_sa_bq': (0.0, 0.8),
     'L0_xattn_sa_bk': (0.0, 0.8),
     'L0_xattn_sa_bv': (0.0, 0.1),
     'L0_xattn_sa_bo': (0.0, 0.1),
     'L0_xattn_ln2_g': (1.0, 0.6),
     'L0_xattn_ln2_b': (0.0, 0.8),
     'L0_xattn_ca_bq': (0.0, 0.8),
     'L0_xattn_ca_bk': (0.0, 0.8),
     'L0_xattn_ca_bv': (0.0, 0.272),
     'L0_xattn_ca_bo': (0.0, 0.1),
     'L0_xattn_ln3_g': (1.0, 0.6),
     'L0_xattn_ln3_b': (0.0, 0.606),
     'L0_xattn_fc1_b': (0.0, 0.1),
     'L0_xattn_fc2_b': (0.0, 0.1),
     'L1_xattn_trans_b': (0.0, 0.1)}
    factors = {'L0_xattn_sa_wq': 8.0, 'L0_xattn_sa_wk': 8.0, 'L0_xattn_ca_wq': 8.0, 'L0_xattn_ca_wk': 8.0}
    for name, (base, spread) in spreads.items():
        noise = np.random.default_rng([zlib.crc32(name.encode()), seed]).standard_normal(out[name].shape)
        drawn = base * np.exp(spread * noise) if base else spread * noise
        out[name] = jnp.asarray(drawn.astype(out[name].dtype))
    for name, factor in factors.items():
        out[name] = (out[name] * factor).astype(out[name].dtype)
    return out
```

```python
from contextlib import ExitStack

import numpy as np
import concourse.bass as bass
from concourse import mybir

F32 = mybir.dt.float32
F32R = mybir.dt.float32r
BF16 = mybir.dt.bfloat16
ALU = mybir.AluOpType
ACT = mybir.ActivationFunctionType
AX_X = mybir.AxisListType.X

P = 128
TILES = 128
E = 256
KC = E // P
H = 16
HD = E // H
FF = 1024
FC = FF // P
G = 4
M = 2
FP = FC // 2
U = 4
FUSE_LAG = 4
EPS = 1e-5
NEG = -3.0e38


def build(nc, d, out_d):
    ctx = ExitStack()
    with ctx:
        def sb(name, shape, dt=F32):
            return ctx.enter_context(nc.sbuf_tensor(name, shape, dt))

        def sem(name):
            return ctx.enter_context(nc.semaphore(name))

        ident = sb("ident", [P, P])
        ident_bf = sb("ident_bf", [P, P], BF16)
        rope_c = sb("rope_c", [P, HD])
        rope_s = sb("rope_s", [P, HD])
        mask_bf = sb("mask_bf", [P, P], BF16)
        mask_t_bf = sb("mask_t_bf", [P, P], BF16)
        dmask = sb("dmask", [P, G])
        ones_f = sb("ones_f", [P, 1])
        mhalf = sb("mhalf", [P, 1])
        eps_t = sb("eps_t", [P, 1])
        dtick = sb("dtick", [P, 1])
        ones_r = sb("ones_r", [P, P], F32R)
        wshapes = {"sqk": (KC, 2 * E), "sv": (KC, E), "so": (KC, E), "ckv": (KC, 2 * E), "cq": (KC, E),
                   "co": (KC, E), "f1": (KC, FF), "f2": (FC, E), "t1": (KC, E), "t2": (KC, E)}
        w_hi = {k: sb(f"w_{k}_hi", [P, *v], F32R) for k, v in wshapes.items()}
        w_lo = {k: sb(f"w_{k}_lo", [P, *v], F32R) for k, v in wshapes.items()}
        ln_g = sb("ln_g", [P, 3, KC])
        ln_b = sb("ln_b", [P, 3, KC])
        bias_sqk = sb("bias_sqk", [P, 2 * E])
        bias_sv = sb("bias_sv", [P, E])
        bias_so = sb("bias_so", [P, E])
        bias_ckv = sb("bias_ckv", [P, 2 * E])
        bias_cq = sb("bias_cq", [P, E])
        bias_co = sb("bias_co", [P, E])
        bias_f2 = sb("bias_f2", [P, E])
        bias_t = sb("bias_t", [P, E])
        bias_f1 = sb("bias_f1", [P, FC])
        rows_in = sb("rows_in", [P, 2 * U, E])
        x_in = [rows_in[:, i, :] for i in range(U)]
        c_in = [rows_in[:, U + i, :] for i in range(U)]
        xt_hi = sb("xt_hi", [P, KC, P], F32R)
        xt_lo = sb("xt_lo", [P, KC, P], F32R)
        ct_hi = [sb(f"ct_hi{i}", [P, KC, P], F32R) for i in range(U)]
        ct_lo = [sb(f"ct_lo{i}", [P, KC, P], F32R) for i in range(U)]
        cw = [sb(f"cw{i}", [P, E]) for i in range(U)]
        x2b_all = sb("x2b_all", [P, U * E])
        x2b = [x2b_all[:, i * E:(i + 1) * E] for i in range(U)]
        vaug = {"s": [sb("vaug_s", [P, H, 2 * HD])] * 2,
                "c": [sb(f"vaug_c{i}", [P, H, 2 * HD]) for i in range(2)]}
        kct_hi = sb("kct_hi", [P, G, P], F32R)
        kct_lo = sb("kct_lo", [P, G, P], F32R)
        skt_hi = sb("skt_hi", [P, G, P], F32R)
        skt_lo = sb("skt_lo", [P, G, P], F32R)
        tqk = sb("tqk", [P, 2 * E])
        qkf = sb("qkf", [P, 2 * E])
        tkc = tqc = sb("tkc", [P, E])
        kcf = sb("kcf", [P, E])
        qcf = sb("qcf", [P, E])
        rsin = sb("rsin", [P, 2 * E])
        kd = sb("kd", [P, H, 2, HD])
        kcd = sb("kcd", [P, H, 2, HD])
        x2t_hi = sb("x2t_hi", [P, KC, P], F32R)
        x2t_lo = sb("x2t_lo", [P, KC, P], F32R)
        h3t_hi = sb("h3t_hi", [P, KC, M * P], F32R)
        h3t_lo = sb("h3t_lo", [P, KC, M * P], F32R)
        hid = [sb(f"hid{i}", [P, 2, M * P]) for i in range(2)]
        hid_hi = sb("hid_hi", [P, FC, M * P], F32R)
        hid_lo = sb("hid_lo", [P, FC, M * P], F32R)
        x3 = sb("x3", [P, E])
        x3t_hi = sb("x3t_hi", [P, KC, P], F32R)
        x3t_lo = sb("x3t_lo", [P, KC, P], F32R)
        fmax = sb("fmax", [P, 1])
        fexp = sb("fexp", [P, P])
        fsum = sb("fsum", [P, 1])
        frec = sb("frec", [P, 1])
        fatt = fexp
        fatt_t = sb("fatt_t", [P, P])
        fpre = sb("fpre", [P, E])
        o_out = [sb(f"o_out{i}", [P, E]) for i in range(2)]
        qs = {c: sb(f"qs_{c}", [P, H, 2, HD], F32R) for c in "sc"}
        qt = dict.fromkeys("sc", sb("qt", [P, G, G, P], F32R))
        nm = {c: sb(f"nm_{c}", [P, G, 32], F32R) for c in "sc"}
        mdiag = dict.fromkeys("sc", sb("mdiag", [P, G, P], F32R))
        pt = dict.fromkeys("sc", sb("pt", [P, G, G, P]))
        stage = [pt["s"][:, :, :, :].rearrange("p b g q -> p (b g q)"), rows_in[:, :, :].rearrange("p r n -> p (r n)")]
        ln_brep = x2b_all[:, 0:3 * KC * P].rearrange("p (l k n) -> p l k n", l=3, k=KC)
        osb = {c: sb(f"osb_{c}", [P, G, P]) for c in "sc"}
        rinv = {c: sb(f"rinv_{c}", [P, H]) for c in "sc"}
        att = dict.fromkeys("sc", sb("att", [P, H, HD]))
        at_hi = dict.fromkeys("sc", sb("at_hi", [P, KC, P], F32R))
        at_lo = dict.fromkeys("sc", sb("at_lo", [P, KC, P], F32R))
        mask_f, mask_tf = osb["s"][:, 0, :], osb["s"][:, 1, :]
        xres = {"s": [sb(f"xres_s{i}", [P, E]) for i in range(2)], "c": [sb("xres_c", [P, E])] * 2}
        x1 = sb("x1", [P, E])
        x2 = sb("x2", [P, E])
        xhat = [sb("xhat0", [P, E])] + [sb("xhat1", [P, E])] * 2
        bst = [sb(f"bst{n}", [P, 6]) for n in range(3)]
        bmv = [sb(f"bmv{n}", [P, 2]) for n in range(3)]
        rstd = [sb(f"rstd{n}", [P, 1]) for n in range(3)]
        sc = ctx.enter_context(nc.psum_tensor("sc", [P, G, 512], F32))
        A0, A1, B0, C0 = [ctx.enter_context(nc.psum_tensor(n, [P, 512], F32)) for n in ("A0", "A1", "B0", "C0")]
        bank_of = {"s": {"q": A0, "m": A1, "pv": A1, "o": B0, "a": B0, "y": B0},
                   "c": {"q": B0, "m": B0, "pv": B0, "o": B0, "a": B0, "y": B0}}

        ld_w = [sem(f"ld_w{i}") for i in range(2)]
        ld_cst = sem("ld_cst")
        st_scaled, st_split, st_cst, st_bmm, st_setup = sem("st_scaled"), sem("st_split"), sem("st_cst"), sem("st_bmm"), sem("st_setup")
        st_ones = sem("st_ones")
        st_hi, st_badd = sem("st_hi"), sem("st_badd")
        ld_x = [sem(f"ld_x{i}") for i in range(G)]
        ld_c = [sem(f"ld_c{i}") for i in range(G)]
        st_o = [sem(f"st_o{i}") for i in range(2)]
        names = ("trx", "trc", "vs", "xt_hi", "xt_lo", "xc_hi", "xc_lo", "qk", "kvc", "vcw", "tqk", "r1", "r2", "qkf", "tkc", "r1k", "r2k", "kcf",
                 "v_s", "v_c", "cw", "kd", "kcd", "trk", "skt_hi", "skt_lo", "trkc", "kct_hi", "kct_lo",
                 "trx2", "x2t_hi", "x2t_lo", "qc", "tqc", "r1q", "r2q", "qcf", "trx3", "h3t_hi", "h3t_lo",
                 "f1", "gelu", "hid_hi", "hid_lo", "f2", "x3", "trf", "x3t_hi", "x3t_lo", "fs", "fmax", "fexp", "frec",
                 "fatt", "trfa", "fatt_t", "fy", "fpre", "ftan", "fout", "x2b")
        s = {n: sem("s_" + n) for n in names}
        per_chain = ("qs_hi", "qs_lo", "trq", "qt", "sc", "nm", "trm", "mdiag", "sct", "exp", "pv", "osb", "tro",
                     "rinv", "att", "tra", "at_hi", "at_lo", "y", "x", "xres")
        sc_ = {c: {n: sem(f"s_{c}_{n}") for n in per_chain} for c in "sc"}
        ln_s = [{n: sem(f"s_ln{k}_{n}") for n in ("st", "mv", "var", "rstd", "xhat")} for k in range(3)]

        BIAS_BANKS = [A0, A1, B0, C0, sc[:, 0, :]]
        F1_BANKS = [A0, B0, A1, C0]

        def tile_of(dram, index):
            if isinstance(index, int):
                return dram[index]
            return dram[bass.ds(index, 1), :, :].rearrange("a p n -> p (a n)")

        def n(at, k=1):
            count = U * at[0] + at[1] + k
            return min(count, TILES) if isinstance(count, int) else count

        def need(eng, sm, count):
            if not isinstance(count, int) or count > 0:
                eng.wait_ge(sm, count)

        def lds(at):
            return 16 * (at[0] + at[1] // U + 1)

        wjobs = [("sqk", "L0_xattn_sa_wq", 0, 0.25, 0, E), ("sqk", "L0_xattn_sa_wk", 0, 1.0, E, E),
                 ("sv", "L0_xattn_sa_wv", 0, 1.0, 0, E), ("so", "L0_xattn_sa_wo", None, 1.0, 0, E),
                 ("ckv", "L0_xattn_ca_wk", None, 1.0, 0, E), ("ckv", "L0_xattn_ca_wv", None, 1.0, E, E),
                 ("cq", "L0_xattn_ca_wq", 1, 0.25, 0, E), ("co", "L0_xattn_ca_wo", None, 1.0, 0, E),
                 ("f1", "L0_xattn_fc1_w", 2, 1.0, 0, FF), ("f2", "L0_xattn_fc2_w", None, 1.0, 0, E),
                 ("t1", "t1", None, 1.0, 0, E), ("t2", "t2", None, 1.0, 0, E)]

        def wview(j):
            name, _, _, _, c0, w = wjobs[j]
            k = wshapes[name][0]
            return (stage[j % 2][:, 0:k * w].rearrange("p (k n) -> p k n", k=k),
                    w_hi[name][:, :, c0:c0 + w], w_lo[name][:, :, c0:c0 + w])

        LN_JOBS = [j for j in range(len(wjobs)) if wjobs[j][2] is not None]
        NBC = 12

        N_CST = 16 * (6 + 6 + 1 + 10)

        def live(at):
            return not isinstance(at[0], int) or 0 <= U * at[0] + at[1] < TILES

        def steps(eng, slot):
            for u in range(U):
                slot(0, u)
            with eng.Fori(1, TILES // U - 1) as i:
                for u in range(U):
                    slot(i, u)
            for u in range(U + FUSE_LAG):
                slot(TILES // U - 1 + u // U, u % U)

        def tiles(i, u):
            return (i, u), (i, u - 1), (i, u - 2), (i, u - FUSE_LAG)

        def group(i, u):
            return 2 * i + u // M if u % M == 1 and live((i, u - 2)) else None

        def before(i, u):
            return 2 * i + u // M - 1

        def read_out(j, groups):
            return FC * (groups - 1) + 2 * (j + 1)

        block = ctx.enter_context(nc.Block())

        @block.sync
        def _(sp):
            def row(dst, name):
                sp.dma_start(dst, d[name].partition_broadcast(P)).then_inc(ld_cst, 16)

            for dst, src in ((ident[:, :], d["c_ident"]), (rope_c[:, :], d["c_rope_c"]), (rope_s[:, :], d["c_rope_s"]),
                             (mask_f, d["c_mask"]), (mask_tf, d["c_mask_t"]), (dmask[:, :], d["c_dmask"])):
                sp.dma_start(dst, src).then_inc(ld_cst, 16)
            for k in range(3):
                sp.dma_start(ln_g[:, k, :], d[f"L0_xattn_ln{k + 1}_g"].rearrange("(k p) -> p k", p=P),
                             allow_slow_non_contiguous=True).then_inc(ld_cst, 16)
                sp.dma_start(ln_b[:, k, :], d[f"L0_xattn_ln{k + 1}_b"].rearrange("(k p) -> p k", p=P),
                             allow_slow_non_contiguous=True).then_inc(ld_cst, 16)
            sp.dma_start(bias_f1[:, :], d["L0_xattn_fc1_b"].rearrange("(k p) -> p k", p=P),
                         allow_slow_non_contiguous=True).then_inc(ld_cst, 16)
            for dst, name in ((bias_sqk[:, 0:E], "L0_xattn_sa_bq"), (bias_sqk[:, E:2 * E], "L0_xattn_sa_bk"),
                              (bias_sv[:, :], "L0_xattn_sa_bv"), (bias_so[:, :], "L0_xattn_sa_bo"),
                              (bias_ckv[:, 0:E], "L0_xattn_ca_bk"), (bias_ckv[:, E:2 * E], "L0_xattn_ca_bv"),
                              (bias_cq[:, :], "L0_xattn_ca_bq"), (bias_co[:, :], "L0_xattn_ca_bo"),
                              (bias_f2[:, :], "L0_xattn_fc2_b"), (bias_t[:, :], "L1_xattn_trans_b")):
                row(dst, name)
            for j in range(len(wjobs)):
                if j >= 2:
                    sp.wait_ge(st_split, j - 1)
                    if j - 2 in LN_JOBS:
                        sp.wait_ge(st_bmm, LN_JOBS.index(j - 2) + 1)
                name, src, _, _, _, w = wjobs[j]
                if name in ("t1", "t2"):
                    src_ap = d["L1_xattn_trans_W"][(name == "t2") * E:(name == "t2") * E + E, :]
                else:
                    src_ap = d[src]
                sp.dma_start(wview(j)[0], src_ap.rearrange("(k p) n -> p k n", p=P)).then_inc(ld_w[j % 2], 16)


            def load(at):
                if not live(at):
                    return
                r = at[1] % U
                src = at[0] * U + at[1]
                need(sp, ln_s[0]["xhat"], n(at, -3))
                need(sp, sc_["s"]["xres"], n(at, -3))
                sp.dma_start(x_in[r], tile_of(d["x"], src)).then_inc(ld_x[r], 16)
                need(sp, s["trc"], n(at, -3))
                sp.dma_start(c_in[r], tile_of(d["ctx_1024"], src)).then_inc(ld_c[r], 16)

            def slot(i, u):
                load((i, u + 2))
                f = tiles(i, u)[3]
                if live(f):
                    sp.wait_ge(s["fout"], n(f))
                    sp.dma_start(tile_of(out_d, f[0] * U + f[1]), o_out[f[1] % 2][:, :]).then_inc(st_o[f[1] % 2], 16)

            sp.wait_ge(st_setup, 1)
            for u in range(2):
                load((0, u))
            steps(sp, slot)
            for q in st_o:
                sp.wait_ge(q, 16 * TILES // 2)

        @block.tensor
        def _(pe):
            pe.wait_ge(st_cst, 1)
            for m, j in enumerate(LN_JOBS):
                pe.wait_ge(ld_w[j % 2], 16 * (j // 2 + 1))
                raw, ln = wview(j)[0], wjobs[j][2]
                if wjobs[j][0] == "f1":
                    for c in range(FC):
                        for k in range(KC):
                            mm = pe.matmul(BIAS_BANKS[m][:, c:c + 1], raw[:, k, c * P:(c + 1) * P], ln_b[:, ln, k:k + 1],
                                           start=(k == 0), stop=(k == KC - 1))
                else:
                    for k in range(KC):
                        mm = pe.matmul(BIAS_BANKS[m][:, 0:E], ln_brep[:, ln, k, :], raw[:, k, :],
                                       start=(k == 0), stop=(k == KC - 1))
                mm.then_inc(st_bmm, 1)
            pe.wait_ge(st_setup, 1)

            def transposes(out, src, count):
                for k in range(count):
                    t = pe.transpose(out[:, k * P:(k + 1) * P], src[:, k * P:(k + 1) * P], ident[:, :])
                return t

            def split3(out, a_hi, a_lo, b_hi, b_lo, k, first, last):
                pe.matmul(out, a_hi, b_hi, start=first, stop=False, skip_group_check=True)
                pe.matmul(out, a_hi, b_lo, start=False, stop=False, skip_group_check=True)
                return pe.matmul(out, a_lo, b_hi, start=False, stop=last, skip_group_check=True)

            def trc(at):
                v = at[1] + 1
                pe.wait_ge(ld_c[at[1] % U], lds(at))
                need(pe, s["kct_hi"], n(at, 0))
                need(pe, s["kct_lo"], n(at, 0))
                if v % M == 0:
                    need(pe, s["gelu"], read_out(0, before(at[0], v)))
                transposes(A0[:, E:2 * E], c_in[at[1] % U], KC).then_inc(s["trc"], 1)

            def trx(at):
                pe.wait_ge(ln_s[0]["xhat"], n(at))
                transposes(A0[:, 0:E], xhat[0][:, :], KC).then_inc(s["trx"], 1)

            def qk(at):
                u = at[1]
                pe.wait_ge(s["xt_hi"], n(at))
                pe.wait_ge(s["xt_lo"], n(at))
                need(pe, sc_["s"]["mdiag"], n(at, 0))
                need(pe, s["skt_hi"], n(at, 0))
                need(pe, s["skt_lo"], n(at, 0))
                for k in range(KC):
                    mm = split3(A1[:, :], xt_hi[:, k, :], xt_lo[:, k, :], w_hi["sqk"][:, k, :],
                                w_lo["sqk"][:, k, :], k, k == 0, k == KC - 1)
                mm.then_inc(s["qk"], 1)

            def vs(at):
                need(pe, s["xc_hi"], n(at, 0))
                need(pe, s["xc_lo"], n(at, 0))
                pe.wait_ge(s["xt_hi"], n(at))
                pe.wait_ge(s["xt_lo"], n(at))
                for k in range(KC):
                    mm = split3(A0[:, 0:E], xt_hi[:, k, :], xt_lo[:, k, :], w_hi["sv"][:, k, :], w_lo["sv"][:, k, :],
                                k, k == 0, False)
                mm.then_inc(s["vs"], 1)

            def vcw(at, alone):
                ch, cl = ct_hi[at[1] % U], ct_lo[at[1] % U]
                pe.wait_ge(s["xc_hi"], n(at))
                pe.wait_ge(s["xc_lo"], n(at))
                for k in range(KC):
                    mm = split3(A0[:, E:2 * E], ch[:, k, :], cl[:, k, :], w_hi["t2"][:, k, :],
                                w_lo["t2"][:, k, :], k, alone and k == 0, k == KC - 1)
                mm.then_inc(s["vcw"], 1)

            def kvc(at):
                ch, cl = ct_hi[at[1] % U], ct_lo[at[1] % U]
                pe.wait_ge(sc_["s"]["osb"], n(at))
                for k in range(KC):
                    mm = split3(A1[:, :], ch[:, k, :], cl[:, k, :], w_hi["ckv"][:, k, :],
                                w_lo["ckv"][:, k, :], k, k == 0, k == KC - 1)
                mm.then_inc(s["kvc"], 1)

            def trq(c, at):
                pe.wait_ge(sc_[c]["qs_hi"], n(at))
                pe.wait_ge(sc_[c]["qs_lo"], n(at))
                if c == "s":
                    pe.wait_ge(s["v_s"], n(at))
                    need(pe, s["cw"], n(at, 0))
                flat = qs[c][:, :, :, :].rearrange("p h s e -> p (h s e)").bitcast(F32)
                transposes(bank_of[c]["q"], flat, G).then_inc(sc_[c]["trq"], 1)

            def trk(at):
                pe.wait_ge(s["kd"], n(at))
                pe.wait_ge(s["tqk"], n(at))
                need(pe, s["tkc"], n(at, 0))
                need(pe, s["v_c"], n(at, 0))
                transposes(A1, kd[:, :, :, :].rearrange("p h s e -> p (h s e)"), G).then_inc(s["trk"], 1)

            def trkc(at):
                pe.wait_ge(s["kcd"], n(at))
                pe.wait_ge(sc_["s"]["qt"], n(at, 2))
                pe.wait_ge(s["cw"], n(at))
                transposes(A0, kcd[:, :, :, :].rearrange("p h s e -> p (h s e)"), G).then_inc(s["trkc"], 1)

            def keys_of(c, at):
                return (skt_hi, skt_lo) if c == "s" else (kct_hi, kct_lo)

            def causal_mask(mask):
                for b in range(G):
                    pe.matmul(sc[:, b, :].rearrange("p (g k) -> p g k", g=G), ident_bf[:, :],
                              mask[:, :].unsqueeze(1).broadcast_to([P, G, P]), start=True, stop=False,
                              skip_group_check=True)

            def scores(c, at):
                kh = keys_of(c, at)[0]
                pe.wait_ge(sc_[c]["qt"], n(at))
                pe.wait_ge(s["skt_hi" if c == "s" else "kct_hi"], n(at))
                if c == "s":
                    need(pe, sc_["c"]["exp"], G * n(at, -1))
                else:
                    pe.wait_ge(sc_["s"]["exp"], G * n(at, 2))
                if c == "s":
                    causal_mask(mask_bf)
                for g in range(G):
                    for b in range(G):
                        mm = pe.matmul(sc[:, g, b * P:(b + 1) * P], qt[c][:, g, b, :], kh[:, g, :],
                                       start=(b == 0 and c == "c"), stop=(b == G - 1), skip_group_check=True)
                    mm.then_inc(sc_[c]["sc"], 1)

            def trm(c, at):
                pe.wait_ge(sc_[c]["nm"], G * n(at))
                if c == "s":
                    pe.wait_ge(s["skt_hi"], n(at))
                    pe.wait_ge(s["skt_lo"], n(at))
                    if (at[1] + 1) % M == 0:
                        need(pe, s["gelu"], read_out(2, before(at[0], at[1] + 1)))
                else:
                    pe.wait_ge(sc_["c"]["qt"], n(at))
                pe.transpose(bank_of[c]["m"][:, 0:P], nm[c][:, :, :].rearrange("p b g -> p (b g)").bitcast(F32),
                             ident[:, :]).then_inc(sc_[c]["trm"], 1)

            def scores_t(c, at):
                kh, kl = keys_of(c, at)
                pe.wait_ge(s["skt_lo" if c == "s" else "kct_lo"], n(at))
                pe.wait_ge(sc_[c]["mdiag"], n(at))
                for g in range(G):
                    pe.matmul(sc[:, g, :], ones_r[32 * g:32 * g + 32, :],
                              mdiag[c][32 * g:32 * g + 32, :, :].rearrange("p b q -> p (b q)"), start=(c == "c"),
                              stop=False, skip_group_check=True)
                for g in range(G):
                    for kk in (kh, kl):
                        mm = pe.matmul(sc[:, g, :], kk[:, g, :], qt[c][:, g, :, :].rearrange("p b q -> p (b q)"),
                                       start=False, stop=(kk is kl), skip_group_check=True)
                    mm.then_inc(sc_[c]["sct"], 1)

            def pv(c, at):
                if c == "s":
                    pe.wait_ge(s["tqk"], n(at, 2))
                pe.wait_ge(s["v_s" if c == "s" else "v_c"], n(at))
                for g in range(G):
                    pe.wait_ge(sc_[c]["exp"], G * n(at, 0) + g + 1)
                    for b in range(G):
                        mm = pe.matmul(bank_of[c]["pv"][32 * b:32 * b + 32, g * P:(g + 1) * P],
                                       vaug[c][at[1] % 2][:, G * g + b, :], pt[c][:, g, b, :], start=True, stop=True,
                                       skip_group_check=True)
                mm.then_inc(sc_[c]["pv"], 1)

            def tro(c, at):
                pe.wait_ge(sc_[c]["osb"], n(at))
                if c == "s":
                    need(pe, s["h3t_hi"], n(at, 0))
                    need(pe, s["h3t_lo"], n(at, 0))
                    if at[1] % M == 0:
                        need(pe, s["gelu"], read_out(1, before(at[0], at[1] + 2)))
                transposes(bank_of[c]["o"], osb[c][:, :, :].rearrange("p g q -> p (g q)"), G).then_inc(sc_[c]["tro"], 1)

            def tra(c, at):
                pe.wait_ge(sc_[c]["att"], n(at))
                transposes(bank_of[c]["a"], att[c][:, :, :].rearrange("p h e -> p (h e)"), KC)\
                    .then_inc(sc_[c]["tra"], 1)

            def y(c, at):
                pe.wait_ge(sc_[c]["at_hi"], n(at))
                pe.wait_ge(sc_[c]["at_lo"], n(at))
                w = "so" if c == "s" else "co"
                for k in range(KC):
                    mm = split3(bank_of[c]["y"][:, 0:E], at_hi[c][:, k, :], at_lo[c][:, k, :], w_hi[w][:, k, :],
                                w_lo[w][:, k, :], k, k == 0, k == KC - 1)
                mm.then_inc(sc_[c]["y"], 1)

            def trx2(at):
                pe.wait_ge(ln_s[1]["xhat"], n(at))
                transposes(B0, xhat[1][:, :], KC).then_inc(s["trx2"], 1)

            def qc(at):
                pe.wait_ge(s["x2t_hi"], n(at))
                pe.wait_ge(s["x2t_lo"], n(at))
                for k in range(KC):
                    mm = split3(B0[:, 0:E], x2t_hi[:, k, :], x2t_lo[:, k, :], w_hi["cq"][:, k, :],
                                w_lo["cq"][:, k, :], k, k == 0, k == KC - 1)
                mm.then_inc(s["qc"], 1)

            def trx3(at):
                pe.wait_ge(ln_s[2]["xhat"], n(at))
                transposes(B0, xhat[2][:, :], KC).then_inc(s["trx3"], 1)

            def f1(i, u):
                gd, (a, k, m, f) = group(i, u), tiles(i, u)
                if gd is None:
                    return
                pe.wait_ge(s["h3t_hi"], n(m))
                pe.wait_ge(s["h3t_lo"], n(m))
                need(pe, s["fpre"], n(f))
                for q in ("kct_hi", "kct_lo", "tkc", "v_c"):
                    pe.wait_ge(s[q], n(k))
                for q in ("skt_hi", "skt_lo"):
                    pe.wait_ge(s[q], n(a))
                for c in range(FC):
                    for kk in range(KC):
                        mm = split3(F1_BANKS[c // 2][:, c % 2 * M * P:(c % 2 + 1) * M * P], w_hi["f1"][:, kk, c * P:(c + 1) * P],
                                    w_lo["f1"][:, kk, c * P:(c + 1) * P], h3t_hi[:, kk, :], h3t_lo[:, kk, :],
                                    kk, kk == 0, kk == KC - 1)
                    if c % 2:
                        mm.then_inc(s["f1"], 1)

            def f2(at):
                j = at[1] % M
                gd = 2 * at[0] + at[1] // M + 1
                pe.wait_ge(s["hid_hi"], FP * gd)
                pe.wait_ge(s["hid_lo"], FP * gd)
                need(pe, s["fpre"], n(at, 0))
                for c in range(FC):
                    mm = split3(C0[:, 0:E], hid_hi[:, c, j * P:(j + 1) * P], hid_lo[:, c, j * P:(j + 1) * P],
                                w_hi["f2"][:, c, :], w_lo["f2"][:, c, :], c, c == 0, c == FC - 1)
                mm.then_inc(s["f2"], 1)

            def trf(at):
                pe.wait_ge(s["x3"], n(at))
                transposes(C0, x3[:, :], KC).then_inc(s["trf"], 1)

            def fs(at):
                pe.wait_ge(s["x3t_hi"], n(at))
                pe.wait_ge(s["x3t_lo"], n(at))
                ch, cl = ct_hi[at[1] % U], ct_lo[at[1] % U]
                for k in range(KC):
                    mm = split3(C0[:, 0:P], x3t_hi[:, k, :], x3t_lo[:, k, :], ch[:, k, :], cl[:, k, :],
                                k, k == 0, k == KC - 1)
                mm.then_inc(s["fs"], 1)

            def trfa(at):
                pe.wait_ge(s["fatt"], n(at))
                pe.transpose(C0[:, 0:P], fatt[:, :], ident[:, :]).then_inc(s["trfa"], 1)

            def fy(at):
                pe.wait_ge(s["fatt_t"], n(at))
                pe.wait_ge(s["cw"], n(at))
                pe.matmul(C0[:, 0:E], fatt_t[:, :], cw[at[1] % U][:, :], start=True, stop=False, skip_group_check=True)
                for k in range(KC):
                    mm = split3(C0[:, 0:E], x3t_hi[:, k, :], x3t_lo[:, k, :], w_hi["t1"][:, k, :],
                                w_lo["t1"][:, k, :], k, False, k == KC - 1)
                mm.then_inc(s["fy"], 1)

            def slot(i, u):
                a, k, m, f = tiles(i, u)
                A, K, X, F = live(a), live(k), live(m), live(f)
                if K: trc(k)
                if A: trx(a)
                if X: tro("s", m)
                if K: trm("s", k)
                if K: causal_mask(mask_t_bf)
                if X: tra("s", m)
                if X: y("s", m)
                if K: scores_t("s", k)
                if X: trx2(m)
                if A: qk(a)
                if X: qc(m)
                if K: pv("s", k)
                if F: f2(f)
                if X: trq("c", m)
                if A: vs(a)
                if K: vcw(k, not A)
                if F: trf(f)
                if K: kvc(k)
                if X: scores("c", m)
                if A: trk(a)
                if F: fs(f)
                if X: trm("c", m)
                if A: trq("s", a)
                if X: scores_t("c", m)
                if F: trfa(f)
                if X: pv("c", m)
                if F: fy(f)
                if X: tro("c", m)
                if X: tra("c", m)
                if K: trkc(k)
                if X: y("c", m)
                if A: scores("s", a)
                if X: trx3(m)
                f1(i, u)

            steps(pe, slot)

        @block.vector
        def _(dve):
            def sub(out, a, hi, signal):
                dve.tensor_tensor(out, a, hi.bitcast(F32), ALU.subtract).then_inc(signal, 1)

            dve.memset(qt["s"][:, :, :, :].bitcast(F32), 0.0)
            dve.memset(nm["s"][:, :, :].bitcast(F32), 0.0)
            dve.memset(nm["c"][:, :, :].bitcast(F32), 0.0)
            for v in (vaug["s"][0], *vaug["c"]):
                dve.memset(v[:, :, HD:2 * HD], 1.0)
            dve.memset(mhalf[:, :], -0.5)
            dve.memset(eps_t[:, :], EPS)
            dve.memset(ones_f[:, :], 1.0).then_inc(st_ones, 1)
            dve.wait_ge(st_ones, 1)
            dve.wait_ge(ld_cst, N_CST)
            dve.tensor_copy(ident_bf[:, :], ident[:, :])
            dve.tensor_copy(mask_bf[:, :], mask_f)
            dve.tensor_copy(mask_t_bf[:, :], mask_tf)
            dve.tensor_copy(ones_r[:, :], ones_f[:, :].broadcast_to([P, P]))
            dve.tensor_copy(ln_brep[:, :, :, :], ln_b[:, :, :].unsqueeze(3).broadcast_to([P, 3, KC, P]))\
                .then_inc(st_cst, 1)
            for j, (name, _, ln, scale, c0, w) in enumerate(wjobs):
                st, hi, lo = wview(j)
                dve.wait_ge(ld_w[j % 2], 16 * (j // 2 + 1))
                if ln is not None:
                    m = LN_JOBS.index(j)
                    dve.wait_ge(st_bmm, m + 1)
                    dst = {"sqk": bias_sqk[:, c0:c0 + E], "sv": bias_sv[:, :], "cq": bias_cq[:, :],
                           "f1": bias_f1[:, :]}[name]
                    nb = FC if name == "f1" else E
                    dve.tensor_tensor(dst, BIAS_BANKS[m][:, 0:nb], dst, ALU.add).then_inc(st_badd, 1)
                    dve.wait_ge(st_badd, m + 1)
                    if scale != 1.0:
                        dve.tensor_scalar(dst, dst, scale, None, ALU.mult)
                    for k in range(KC):
                        last = dve.tensor_scalar(st[:, k, :], st[:, k, :], ln_g[:, ln, k:k + 1], scale,
                                                 ALU.mult, ALU.mult)
                    last.then_inc(st_scaled, 1)
                    dve.wait_ge(st_scaled, m + 1)
                dve.tensor_copy(hi, st).then_inc(st_hi, 1)
                dve.wait_ge(st_hi, j + 1)
                dve.tensor_tensor(lo, st, hi.bitcast(F32), ALU.subtract).then_inc(st_split, 1)
            dve.drain().then_inc(st_setup, 1)

            def layernorm(k, src, at, meanwhile=None):
                q = ln_s[k]
                dve.bn_stats(bst[k][:, :], src).then_inc(q["st"], 1)
                dve.wait_ge(q["st"], n(at))
                dve.tensor_copy(dtick[:, :], eps_t[:, :])
                dve.bn_aggr(bmv[k][:, :], bst[k][:, :]).then_inc(q["mv"], 1)
                if meanwhile:
                    maxima("s", meanwhile, (0,))
                dve.wait_ge(q["rstd"], n(at))
                dve.tensor_scalar(xhat[k][:, :], src, bmv[k][:, 0:1], rstd[k][:, 0:1], ALU.subtract, ALU.mult)\
                    .then_inc(q["xhat"], 1)

            def ln1(at):
                if not live(at):
                    return
                dve.wait_ge(ld_x[at[1] % U], lds(at))
                need(dve, s["trx"], n(at, 0))
                layernorm(0, x_in[at[1] % U], at)

            def xt_lo_(at):
                dve.wait_ge(s["xt_hi"], n(at))
                need(dve, s["xc_hi"], n(at, 0))
                need(dve, s["vs"], n(at, 0))
                sub(xt_lo[:, :, :], A0[:, 0:E].rearrange("p (k q) -> p k q", q=P), xt_hi[:, :, :], s["xt_lo"])

            def ct_lo_(at):
                u = at[1]
                dve.wait_ge(s["xc_hi"], n(at))
                dve.wait_ge(s["xt_hi"], n(at, 2))
                need(dve, s["fs"], n(at, -3))
                sub(ct_lo[u % U][:, :, :], A0[:, E:2 * E].rearrange("p (k q) -> p k q", q=P), ct_hi[u % U][:, :, :],
                    s["xc_lo"])

            def rotate(out2, src, sig, width):
                v = src.rearrange("p (h s e) -> p h s e", s=2, e=HD // 2)
                o = out2.rearrange("p (h s e) -> p h s e", s=2, e=HD // 2)
                nh = width // HD
                for half in range(2):
                    w = dve.tensor_tensor(o[:, :, half, :], v[:, :, 1 - half, :],
                                          rope_s[:, half * 8:half * 8 + 8].unsqueeze(1).broadcast_to([P, nh, 8]),
                                          ALU.mult)
                w.then_inc(sig, 1)

            def bias_add(at, out, bank, bias, ready, signal, used=(), count=0):
                dve.wait_ge(ready, n(at))
                for q in used:
                    need(dve, q, count)
                dve.tensor_tensor(out, bank, bias, ALU.add).then_inc(signal, 1)

            def rope(at, t, out, width, sig_t, sig_a, sig_b, sig_o, rsin_used, count):
                dve.wait_ge(sig_t, n(at))
                need(dve, rsin_used, count)
                rotate(rsin[:, 0:width], t[:, :], sig_b, width)
                dve.wait_ge(sig_b, n(at))
                dve.wait_ge(sig_a, n(at))
                dve.tensor_tensor(out[:, :], out[:, :], rsin[:, 0:width], ALU.add).then_inc(sig_o, 1)

            def v_s(at):
                need(dve, sc_["s"]["pv"], n(at, 0))
                dve.wait_ge(s["vs"], n(at))
                need(dve, s["vcw"], n(at, 0))
                dve.tensor_tensor(vaug["s"][at[1] % 2][:, :, 0:HD], A0[:, 0:E].rearrange("p (h e) -> p h e", e=HD),
                                  bias_sv[:, :].rearrange("p (h e) -> p h e", e=HD), ALU.add).then_inc(s["v_s"], 1)

            def v_c(at):
                need(dve, sc_["c"]["pv"], n(at, -1))
                dve.wait_ge(s["kvc"], n(at))
                dve.tensor_tensor(vaug["c"][at[1] % 2][:, :, 0:HD], A1[:, E:2 * E].rearrange("p (h e) -> p h e", e=HD),
                                  bias_ckv[:, E:2 * E].rearrange("p (h e) -> p h e", e=HD), ALU.add)\
                    .then_inc(s["v_c"], 1)

            def qs_lo(c, at):
                dve.wait_ge(sc_[c]["qs_hi"], n(at))
                src = (qkf[:, 0:E] if c == "s" else qcf[:, :]).rearrange("p (h e) -> p h e", e=HD)
                sub(qs[c][:, :, 1, :], src, qs[c][:, :, 0, :], sc_[c]["qs_lo"])

            def skt_lo_(at):
                dve.wait_ge(s["skt_hi"], n(at))
                sub(skt_lo[:, :, :], A1[:, :].rearrange("p (k q) -> p k q", q=P), skt_hi[:, :, :], s["skt_lo"])

            def kct_lo_(at):
                dve.wait_ge(s["kct_hi"], n(at))
                sub(kct_lo[:, :, :], A0[:, :].rearrange("p (k q) -> p k q", q=P), kct_hi[:, :, :], s["kct_lo"])

            def maxima(c, at, groups):
                for g in groups:
                    dve.wait_ge(sc_[c]["sc"], G * n(at, 0) + g + 1)
                    dve.tensor_reduce(nm[c][:, g, 0:G], sc[:, g, :].rearrange("p (b k) -> p b k", b=G),
                                      AX_X, ALU.max, negate=True).then_inc(sc_[c]["nm"], 1)

            def mdiag_(c, at):
                dve.wait_ge(sc_[c]["trm"], n(at))
                dve.tensor_tensor(mdiag[c][:, :, :], bank_of[c]["m"][:, 0:P].unsqueeze(1).broadcast_to([P, G, P]),
                                  dmask[:, :].unsqueeze(2).broadcast_to([P, G, P]), ALU.mult)\
                    .then_inc(sc_[c]["mdiag"], 1)

            def normalise(c, at):
                bank = bank_of[c]["o"][:, :].rearrange("p (h s) -> p h s", s=2 * HD)
                dve.wait_ge(sc_[c]["tro"], n(at))
                dve.reciprocal(rinv[c][:, :], bank[:, :, HD]).then_inc(sc_[c]["rinv"], 1)
                dve.wait_ge(sc_[c]["rinv"], n(at))
                dve.tensor_tensor(att[c][:, :, :], bank[:, :, 0:HD],
                                  rinv[c][:, :].unsqueeze(2).broadcast_to([P, H, HD]), ALU.mult)\
                    .then_inc(sc_[c]["att"], 1)

            def at_hi_(c, at):
                dve.wait_ge(sc_[c]["tra"], n(at))
                dve.tensor_copy(at_hi[c][:, :, :], bank_of[c]["a"][:, 0:E].rearrange("p (k q) -> p k q", k=KC))\
                    .then_inc(sc_[c]["at_hi"], 1)

            def at_lo_(c, at):
                dve.wait_ge(sc_[c]["at_hi"], n(at))
                sub(at_lo[c][:, :, :], bank_of[c]["a"][:, 0:E].rearrange("p (k q) -> p k q", k=KC), at_hi[c][:, :, :],
                    sc_[c]["at_lo"])

            def residual(c, at, meanwhile=None):
                dst = x1 if c == "s" else x2
                dve.wait_ge(sc_[c]["xres"], n(at))
                dve.wait_ge(sc_[c]["y"], n(at))
                nxt = s["x2b"] if c == "c" else sc_["c"]["xres"]
                need(dve, nxt, n(at, 0))
                dve.tensor_tensor(dst[:, :], bank_of[c]["y"][:, 0:E], xres[c][at[1] % 2][:, :], ALU.add)\
                    .then_inc(sc_[c]["x"], 1)
                dve.wait_ge(sc_[c]["x"], n(at))
                layernorm(1 if c == "s" else 2, dst[:, :], at, meanwhile)

            def x2t_lo_(at):
                dve.wait_ge(s["x2t_hi"], n(at))
                sub(x2t_lo[:, :, :], B0[:, 0:E].rearrange("p (k q) -> p k q", k=KC), x2t_hi[:, :, :], s["x2t_lo"])

            def h3t_lo_(at):
                j = at[1] % M
                dve.wait_ge(s["h3t_hi"], n(at))
                sub(h3t_lo[:, :, j * P:(j + 1) * P], B0[:, 0:E].rearrange("p (k q) -> p k q", k=KC),
                    h3t_hi[:, :, j * P:(j + 1) * P], s["h3t_lo"])

            def hid_lo_(i, u):
                gd = group(i, u)
                if gd is None:
                    return
                for c in range(FP):
                    dve.wait_ge(s["hid_hi"], FP * (gd - 1) + c + 1)
                    sub(hid_lo[:, 2 * c:2 * c + 2, :], hid[c % 2][:, :, :], hid_hi[:, 2 * c:2 * c + 2, :], s["hid_lo"])

            def x3_(at):
                dve.wait_ge(s["f2"], n(at))
                dve.wait_ge(s["x2b"], n(at))
                need(dve, s["fout"], n(at, 0))
                dve.tensor_tensor(x3[:, :], C0[:, 0:E], x2b[at[1] % U][:, :], ALU.add).then_inc(s["x3"], 1)

            def x3t_lo_(at):
                dve.wait_ge(s["x3t_hi"], n(at))
                sub(x3t_lo[:, :, :], C0[:, 0:E].rearrange("p (k q) -> p k q", k=KC), x3t_hi[:, :, :], s["x3t_lo"])

            def fmax_(at):
                dve.wait_ge(s["fs"], n(at))
                dve.tensor_reduce(fmax[:, :], C0[:, 0:P], AX_X, ALU.max, negate=True).then_inc(s["fmax"], 1)

            def fatt_(at):
                dve.wait_ge(s["fexp"], n(at))
                dve.reciprocal(frec[:, :], fsum[:, :]).then_inc(s["frec"], 1)
                dve.wait_ge(s["frec"], n(at))
                dve.tensor_scalar(fatt[:, :], fexp[:, :], frec[:, 0:1], None, ALU.mult).then_inc(s["fatt"], 1)

            def fpre_(at):
                dve.wait_ge(s["fy"], n(at))
                need(dve, s["fout"], n(at, 0))
                dve.tensor_tensor(fpre[:, :], C0[:, 0:E], bias_t[:, :], ALU.add).then_inc(s["fpre"], 1)

            def slot(i, u):
                a, k, m, f = tiles(i, u)
                A, K, X, F = live(a), live(k), live(m), live(f)
                if X: normalise("s", m)
                if K: mdiag_("s", k)
                if X: at_lo_("s", m)
                if A: xt_lo_(a)
                if K: ct_lo_(k)
                if X: residual("s", m)
                if X: x2t_lo_(m)
                if A: bias_add(a, tqk[:, :], A1[:, :], bias_sqk[:, :], s["qk"], s["tqk"])
                if X: bias_add(m, tqc[:, :], B0[:, 0:E], bias_cq[:, :], s["qc"], s["tqc"], (s["r1k"], s["r2k"]), n(m))
                if X: rope(m, tqc, qcf, E, s["tqc"], s["r1q"], s["r2q"], s["qcf"], s["kcf"], n(m))
                if X: qs_lo("c", m)
                if A: rope(a, tqk, qkf, 2 * E, s["tqk"], s["r1"], s["r2"], s["qkf"], s["qcf"], n(a, -1))
                if F: x3_(f)
                if A: v_s(a)
                if K: bias_add(k, tkc[:, :], A1[:, 0:E], bias_ckv[:, 0:E], s["kvc"], s["tkc"], (s["r1q"], s["r2q"]), n(k, 0))
                if K: v_c(k)
                if F: x3t_lo_(f)
                if A: qs_lo("s", a)
                if X: maxima("c", m, range(G))
                if A: skt_lo_(a)
                if X: mdiag_("c", m)
                if K: rope(k, tkc, kcf, E, s["tkc"], s["r1k"], s["r2k"], s["kcf"], s["qkf"], n(k, 2))
                if F: fmax_(f)
                if F: fatt_(f)
                ln1((i, u + 1))
                if F: fpre_(f)
                if X: normalise("c", m)
                if X: at_hi_("c", m)
                if X: at_lo_("c", m)
                if K: kct_lo_(k)
                if X: residual("c", m, a if A else None)
                if A: maxima("s", a, (1,) if X else (0, 1))
                if X: h3t_lo_(m)
                if A: maxima("s", a, (2, 3))
                hid_lo_(i, u)

            ln1((0, 0))
            steps(dve, slot)

        @block.scalar
        def _(act):
            act.wait_ge(st_setup, 1)

            def copy(out, src, signal):
                act.copy(out, src).then_inc(signal, 1)

            def xt_hi_(at):
                act.wait_ge(s["trx"], n(at))
                need(act, s["trc"], n(at, 0))
                need(act, s["vs"], n(at, 0))
                copy(xt_hi[:, :, :], A0[:, 0:E].rearrange("p (k q) -> p k q", q=P), s["xt_hi"])

            def ct_hi_(at):
                act.wait_ge(s["trc"], n(at))
                act.wait_ge(s["trx"], n(at, 2))
                need(act, s["fs"], n(at, -3))
                copy(ct_hi[at[1] % U][:, :, :], A0[:, E:2 * E].rearrange("p (k q) -> p k q", q=P), s["xc_hi"])

            def qs_hi(c, at):
                act.wait_ge(s["qkf" if c == "s" else "qcf"], n(at))
                need(act, sc_[c]["trq"], n(at, 0))
                src = (qkf[:, 0:E] if c == "s" else qcf[:, :]).rearrange("p (h e) -> p h e", e=HD)
                copy(qs[c][:, :, 0, :], src, sc_[c]["qs_hi"])

            def twice(dst, src, at, ready, used, signal):
                act.wait_ge(ready, n(at))
                need(act, used, n(at, 0))
                v = src.rearrange("p (h e) -> p h e", e=HD).unsqueeze(2).broadcast_to([P, H, 2, HD])
                copy(dst[:, :, :, :], v, signal)

            def qt_(c, at):
                act.wait_ge(sc_[c]["trq"], n(at))
                if c == "s":
                    need(act, sc_["c"]["sct"], G * n(at, -1))
                else:
                    act.wait_ge(sc_["s"]["sct"], G * n(at, 2))
                for b in range(G):
                    part = slice(32 * b, 32 * b + 32)
                    w = act.copy(qt[c][part, :, b, :], bank_of[c]["q"][part, :].rearrange("p (g q) -> p g q", q=P))
                w.then_inc(sc_[c]["qt"], 1)

            def skt_hi_(at):
                act.wait_ge(s["trk"], n(at))
                need(act, sc_["s"]["sct"], G * n(at, 0))
                copy(skt_hi[:, :, :], A1[:, :].rearrange("p (k q) -> p k q", q=P), s["skt_hi"])

            def kct_hi_(at):
                act.wait_ge(s["trkc"], n(at))
                need(act, sc_["c"]["sct"], G * n(at, 0))
                copy(kct_hi[:, :, :], A0[:, :].rearrange("p (k q) -> p k q", q=P), s["kct_hi"])

            def cw_(at):
                act.wait_ge(s["vcw"], n(at))
                act.wait_ge(s["v_s"], n(at, 2))
                need(act, s["fy"], n(at, -3))
                copy(cw[at[1] % U][:, :], A0[:, E:2 * E], s["cw"])

            def exps(c, at):
                if c == "s":
                    need(act, sc_["c"]["pv"], n(at, -1))
                else:
                    act.wait_ge(sc_["s"]["pv"], n(at, 2))
                for g in range(G):
                    act.wait_ge(sc_[c]["sct"], G * n(at, 0) + g + 1)
                    act.activation(pt[c][:, g, :, :].rearrange("p b q -> p (b q)"), sc[:, g, :], ACT.Exp)\
                       .then_inc(sc_[c]["exp"], 1)

            def osb_(c, at):
                act.wait_ge(sc_[c]["pv"], n(at))
                copy(osb[c][:, :, :].rearrange("p g q -> p (g q)"), bank_of[c]["pv"][:, :], sc_[c]["osb"])

            def at_hi_(c, at):
                act.wait_ge(sc_[c]["tra"], n(at))
                copy(at_hi[c][:, :, :], bank_of[c]["a"][:, 0:E].rearrange("p (k q) -> p k q", k=KC), sc_[c]["at_hi"])

            def x2t_hi_(at):
                act.wait_ge(s["trx2"], n(at))
                copy(x2t_hi[:, :, :], B0[:, 0:E].rearrange("p (k q) -> p k q", k=KC), s["x2t_hi"])

            def h3t_hi_(at):
                j = at[1] % M
                act.wait_ge(s["trx3"], n(at))
                if j == 0:
                    need(act, s["f1"], FP * (2 * at[0] + at[1] // M))
                copy(h3t_hi[:, :, j * P:(j + 1) * P], B0[:, 0:E].rearrange("p (k q) -> p k q", k=KC), s["h3t_hi"])

            def gelus(i, u):
                gd = group(i, u)
                if gd is None:
                    return
                for c in range(FC):
                    m = FP * (gd - 1) + c // 2 + 1
                    act.wait_ge(s["f1"], m)
                    need(act, s["hid_lo"], m - 2)
                    act.activation(hid[c // 2 % 2][:, c % 2, :], F1_BANKS[c // 2][:, c % 2 * M * P:(c % 2 + 1) * M * P],
                                   ACT.Gelu_apprx_tanh, bias=bias_f1[:, c:c + 1]).then_inc(s["gelu"], 1)

            def x3t_hi_(at):
                act.wait_ge(s["trf"], n(at))
                copy(x3t_hi[:, :, :], C0[:, 0:E].rearrange("p (k q) -> p k q", k=KC), s["x3t_hi"])

            def fexp_(at):
                act.wait_ge(s["fmax"], n(at))
                act.activation(fexp[:, :], C0[:, 0:P], ACT.Exp, bias=fmax[:, 0:1], accum_out=fsum[:, :])\
                   .then_inc(s["fexp"], 1)

            def fatt_t_(at):
                act.wait_ge(s["trfa"], n(at))
                copy(fatt_t[:, :], C0[:, 0:P], s["fatt_t"])

            def ftan_(at):
                act.wait_ge(s["fpre"], n(at))
                act.activation(fpre[:, :], fpre[:, :], ACT.Tanh).then_inc(s["ftan"], 1)

            def slot(i, u):
                a, k, m, f = tiles(i, u)
                A, K, X, F = live(a), live(k), live(m), live(f)
                if A: xt_hi_(a)
                if K: ct_hi_(k)
                if X: at_hi_("s", m)
                if K: exps("s", k)
                if X: x2t_hi_(m)
                if K: osb_("s", k)
                if X: qs_hi("c", m)
                if X: qt_("c", m)
                if F: x3t_hi_(f)
                if K: cw_(k)
                if A: qs_hi("s", a)
                if A: twice(kd, qkf[:, E:2 * E], a, s["qkf"], s["trk"], s["kd"])
                if A: skt_hi_(a)
                if F: fexp_(f)
                if K: twice(kcd, kcf[:, :], k, s["kcf"], s["trkc"], s["kcd"])
                if X: exps("c", m)
                if F: fatt_t_(f)
                if X: osb_("c", m)
                if A: qt_("s", a)
                if K: kct_hi_(k)
                if F: ftan_(f)
                if X: h3t_hi_(m)
                gelus(i, u)

            steps(act, slot)

        @block.gpsimd
        def _(pool):
            pool.wait_ge(st_setup, 1)

            def cosines(at, out, t, width, ready, signal, used, used2):
                pool.wait_ge(ready, n(at))
                need(pool, used, n(at, 0))
                if used2:
                    need(pool, used2, n(at, 0))
                nh = width // HD
                pool.tensor_tensor(out[:, :].rearrange("p (h e) -> p h e", e=HD),
                                   t[:, :].rearrange("p (h e) -> p h e", e=HD),
                                   rope_c[:, :].unsqueeze(1).broadcast_to([P, nh, HD]), ALU.mult).then_inc(signal, 1)

            def rstd_(k, at):
                if not live(at):
                    return
                q = ln_s[k]
                pool.wait_ge(q["mv"], n(at))
                pool.tensor_tensor(rstd[k][:, :], bmv[k][:, 1:2], eps_t[:, :], ALU.add).then_inc(q["var"], 1)
                pool.wait_ge(q["var"], n(at))
                pool.tensor_tensor(rstd[k][:, :], rstd[k][:, :], mhalf[:, :], ALU.pow).then_inc(q["rstd"], 1)

            def xres_s(at):
                if not live(at):
                    return
                pool.wait_ge(ld_x[at[1] % U], lds(at))
                need(pool, sc_["s"]["x"], n(at, -1))
                pool.tensor_tensor(xres["s"][at[1] % 2][:, :], x_in[at[1] % U], bias_so[:, :], ALU.add)\
                    .then_inc(sc_["s"]["xres"], 1)

            def xres_c(at):
                pool.wait_ge(sc_["s"]["x"], n(at))
                need(pool, sc_["c"]["x"], n(at, 0))
                pool.tensor_tensor(xres["c"][at[1] % 2][:, :], x1[:, :], bias_co[:, :], ALU.add)\
                    .then_inc(sc_["c"]["xres"], 1)

            def x2b_(at):
                pool.wait_ge(sc_["c"]["x"], n(at))
                need(pool, s["x3"], n(at, -1))
                pool.tensor_tensor(x2b[at[1] % U][:, :], x2[:, :], bias_f2[:, :], ALU.add).then_inc(s["x2b"], 1)

            def hid_hi_(i, u):
                gd = group(i, u)
                if gd is None:
                    return
                need(pool, s["f2"], n((i, u - FUSE_LAG)))
                for c in range(FP):
                    pool.wait_ge(s["gelu"], FC * (gd - 1) + 2 * c + 2)
                    pool.tensor_tensor(hid_hi[:, 2 * c:2 * c + 2, :], hid[c % 2][:, :, :],
                                       ones_f[:, :].unsqueeze(1).broadcast_to([P, 2, M * P]), ALU.mult).then_inc(s["hid_hi"], 1)

            def fout_(at):
                pool.wait_ge(s["ftan"], n(at))
                need(pool, st_o[at[1] % 2], 16 * (2 * at[0] + at[1] // 2))
                pool.tensor_tensor(o_out[at[1] % 2][:, :], fpre[:, :], x3[:, :], ALU.add).then_inc(s["fout"], 1)

            def slot(i, u):
                a, k, m, f = tiles(i, u)
                A, K, X, F = live(a), live(k), live(m), live(f)
                if X: rstd_(1, m)
                if X: xres_c(m)
                if X: cosines(m, qcf, tqc, E, s["tqc"], s["r1q"], sc_["c"]["qs_lo"], None)
                if A: cosines(a, qkf, tqk, 2 * E, s["tqk"], s["r1"], sc_["s"]["qs_lo"], s["kd"])
                if K: cosines(k, kcf, tkc, E, s["tkc"], s["r1k"], s["kcd"], None)
                if K: xres_s(k)
                rstd_(0, (i, u + 1))
                if F: fout_(f)
                if X: rstd_(2, m)
                if X: x2b_(m)
                hid_hi_(i, u)

            rstd_(0, (0, 0))
            steps(pool, slot)


def shape_constants():
    f = np.float32
    inv = (f(1.0) / f(10000.0) ** (np.arange(0, HD, 2, dtype=f) / f(HD))).astype(f)
    ang = np.outer(np.arange(P, dtype=f), inv).astype(f).astype(np.float64)
    cos, sin = np.cos(ang).astype(f), np.sin(ang).astype(f)
    p = np.arange(P)
    return {
        "c_ident": np.eye(P, dtype=f),
        "c_rope_c": np.concatenate([cos, cos], 1),
        "c_rope_s": np.concatenate([-sin, sin], 1),
        "c_mask": np.where(p[None, :] <= p[:, None], 0.0, NEG).astype(f),
        "c_mask_t": np.where(p[None, :] >= p[:, None], 0.0, NEG).astype(f),
        "c_dmask": (p[:, None] % 32 == np.arange(G)[None, :]).astype(f),
    }


def kernel(**inputs):
    import concourse.bacc as bacc
    from concourse.bass_utils import run_bass_kernel_spmd

    nc = bacc.Bacc("TRN2", target_bir_lowering=False, num_devices=1)
    arrays, d = {}, {}
    for name, a in {**inputs, **shape_constants()}.items():
        arrays[f"in_{name}"] = np.ascontiguousarray(a)
        d[name] = nc.dram_tensor(f"in_{name}", arrays[f"in_{name}"].shape, F32, kind="ExternalInput").ap()
    out_d = nc.dram_tensor("out_0", (TILES, P, E), F32, kind="ExternalOutput").ap()
    build(nc, d, out_d)
    return run_bass_kernel_spmd(nc, [arrays], core_ids=[0]).results[0]["out_0"]
```
